# Optimizing a Trainium2 kernel written in Bass

```python
import numpy as np
import jax
import jax.numpy as jnp

def _softmax(x, axis=-1):
    return jax.nn.softmax(x, axis=axis)

def _gelu(x):
    return jax.nn.gelu(x, approximate=True)

def _silu(x):
    return jax.nn.silu(x)

def _sigmoid(x):
    return jax.nn.sigmoid(x)

def _layernorm(x, axis=-1, eps=1e-05):
    m = jnp.mean(x, axis=axis, keepdims=True)
    v = jnp.var(x, axis=axis, keepdims=True)
    return (x - m) / jnp.sqrt(v + eps)

def _scatter_add(tgt, idx, src, axis=0):
    return tgt.at[idx].add(src)

def _segment_sum(src, seg, n):
    return jax.ops.segment_sum(src, seg, n)
kernel_name = 'mk_seq_preln_d1_jaxref_r4_8eaccd'

def setup_inputs(seed: int=0):
    np.random.seed(seed)
    _w = jnp.asarray

    def _L0_attn_setup():
        import jax, jax.numpy as jnp
        import numpy as np
        DIM = 256
        N_STATE = 64
        DT_RANK = 64
        EPS = 1e-05

        def _forward(x, ln_w, ln_b, w_xproj, w_dt, b_dt, A_log, Dp, w_out):
            B, L, D = x.shape
            mu = jnp.mean(x, axis=-1, keepdims=True)
            var = jnp.var(x, axis=-1, keepdims=True)
            xn = (x - mu) / jnp.sqrt(var + EPS) * ln_w + ln_b
            proj = xn @ w_xproj
            dtr = proj[..., :DT_RANK]
            B_ssm = proj[..., DT_RANK:DT_RANK + N_STATE]
            C_ssm = proj[..., DT_RANK + N_STATE:]
            delta = jax.nn.softplus(dtr @ w_dt + b_dt)
            A = -jnp.exp(A_log)

            def step(h, inp):
                dt, bt, xt, ct = inp
                dA = jnp.exp(dt[..., None] * A)
                h = dA * h + (dt * xt)[..., None] * bt[:, None, :]
                y = jnp.einsum('bdn,bn->bd', h, ct)
                return (h, y)
            h0 = jnp.zeros((B, D, N_STATE), x.dtype)
            xs = (jnp.swapaxes(delta, 0, 1), jnp.swapaxes(B_ssm, 0, 1), jnp.swapaxes(xn, 0, 1), jnp.swapaxes(C_ssm, 0, 1))
            _, ys = jax.lax.scan(step, h0, xs)
            y = jnp.swapaxes(ys, 0, 1)
            return (y + x * Dp) @ w_out
        key = jax.random.key(seed)
        ks = jax.random.split(key, 5)
        B, L = (2, 1024)
        x = jax.random.normal(ks[0], (B, L, DIM), jnp.float32)
        ln_w = jnp.ones((DIM,), jnp.float32)
        ln_b = jnp.zeros((DIM,), jnp.float32)
        w_xproj = jax.random.normal(ks[1], (DIM, DT_RANK + 2 * N_STATE), jnp.float32) * 0.02
        w_dt = jax.random.normal(ks[2], (DT_RANK, DIM), jnp.float32) * 0.02
        b_dt = jnp.zeros((DIM,), jnp.float32)
        A_log = jnp.broadcast_to(jnp.log(jnp.arange(1, N_STATE + 1, dtype=jnp.float32))[None, :], (DIM, N_STATE)) + 0.0
        Dp = jnp.ones((DIM,), jnp.float32)
        w_out = jax.random.normal(ks[3], (DIM, DIM), jnp.float32) * 0.02
        return {'x': x, 'ln_w': ln_w, 'ln_b': ln_b, 'w_xproj': w_xproj, 'w_dt': w_dt, 'b_dt': b_dt, 'A_log': A_log, 'Dp': Dp, 'w_out': w_out}
    _L0_attn_in = _L0_attn_setup()

    def _L0_ffn_setup():
        import jax, jax.numpy as jnp
        import numpy as np
        D_MODEL = 256
        M = 64
        INNER = 16
        key = jax.random.key(seed)
        ks = jax.random.split(key, 9)

        def init(k, shape, fan_in):
            bound = 1.0 / np.sqrt(fan_in)
            return jax.random.uniform(k, shape, jnp.float32, -bound, bound)
        x = jax.random.normal(ks[0], (16, 1024, D_MODEL), dtype=jnp.float32)
        Win = init(ks[1], (D_MODEL, M), D_MODEL)
        bin_ = init(ks[2], (M,), D_MODEL)
        W1 = init(ks[3], (M, INNER), 1)
        b1 = init(ks[4], (M, INNER), 1)
        W2 = init(ks[5], (M, INNER), INNER)
        b2 = init(ks[6], (M,), INNER)
        Wout = init(ks[7], (M, D_MODEL), M)
        bout = init(ks[8], (D_MODEL,), M)
        return {'x': x, 'Win': Win, 'bin_': bin_, 'W1': W1, 'b1': b1, 'W2': W2, 'b2': b2, 'Wout': Wout, 'bout': bout}
    _L0_ffn_in = _L0_ffn_setup()
    _d = {'L0_attn_x': _L0_attn_in['x'], 'L0_attn_ln_w': _L0_attn_in['ln_w'], 'L0_attn_ln_b': _L0_attn_in['ln_b'], 'L0_attn_w_xproj': _L0_attn_in['w_xproj'], 'L0_attn_w_dt': _L0_attn_in['w_dt'], 'L0_attn_b_dt': _L0_attn_in['b_dt'], 'L0_attn_A_log': _L0_attn_in['A_log'], 'L0_attn_Dp': _L0_attn_in['Dp'], 'L0_attn_w_out': _L0_attn_in['w_out'], 'L0_ffn_Win': _L0_ffn_in['Win'], 'L0_ffn_bin_': _L0_ffn_in['bin_'], 'L0_ffn_W1': _L0_ffn_in['W1'], 'L0_ffn_b1': _L0_ffn_in['b1'], 'L0_ffn_W2': _L0_ffn_in['W2'], 'L0_ffn_b2': _L0_ffn_in['b2'], 'L0_ffn_Wout': _L0_ffn_in['Wout'], 'L0_ffn_bout': _L0_ffn_in['bout']}
    _x0 = _d['L0_attn_x']
    _d['L0_attn_x'] = jax.random.normal(jax.random.fold_in(jax.random.key(seed), 1), (32, 512, 256), dtype=_x0.dtype)
    del _x0
    return _d

def reference(L0_attn_x, L0_attn_ln_w, L0_attn_ln_b, L0_attn_w_xproj, L0_attn_w_dt, L0_attn_b_dt, L0_attn_A_log, L0_attn_Dp, L0_attn_w_out, L0_ffn_Win, L0_ffn_bin_, L0_ffn_W1, L0_ffn_b1, L0_ffn_W2, L0_ffn_b2, L0_ffn_Wout, L0_ffn_bout):

    def _L0_attn_ref(x, ln_w, ln_b, w_xproj, w_dt, b_dt, A_log, Dp, w_out):
        import jax, jax.numpy as jnp
        import numpy as np
        DIM = 256
        N_STATE = 64
        DT_RANK = 64
        EPS = 1e-05

        def _forward(x, ln_w, ln_b, w_xproj, w_dt, b_dt, A_log, Dp, w_out):
            B, L, D = x.shape
            mu = jnp.mean(x, axis=-1, keepdims=True)
            var = jnp.var(x, axis=-1, keepdims=True)
            xn = (x - mu) / jnp.sqrt(var + EPS) * ln_w + ln_b
            proj = xn @ w_xproj
            dtr = proj[..., :DT_RANK]
            B_ssm = proj[..., DT_RANK:DT_RANK + N_STATE]
            C_ssm = proj[..., DT_RANK + N_STATE:]
            delta = jax.nn.softplus(dtr @ w_dt + b_dt)
            A = -jnp.exp(A_log)

            def step(h, inp):
                dt, bt, xt, ct = inp
                dA = jnp.exp(dt[..., None] * A)
                h = dA * h + (dt * xt)[..., None] * bt[:, None, :]
                y = jnp.einsum('bdn,bn->bd', h, ct)
                return (h, y)
            h0 = jnp.zeros((B, D, N_STATE), x.dtype)
            xs = (jnp.swapaxes(delta, 0, 1), jnp.swapaxes(B_ssm, 0, 1), jnp.swapaxes(xn, 0, 1), jnp.swapaxes(C_ssm, 0, 1))
            _, ys = jax.lax.scan(step, h0, xs)
            y = jnp.swapaxes(ys, 0, 1)
            return (y + x * Dp) @ w_out
        return _forward(x, ln_w, ln_b, w_xproj, w_dt, b_dt, A_log, Dp, w_out)

    def _L0_ffn_ref(x, Win, bin_, W1, b1, W2, b2, Wout, bout):
        import jax, jax.numpy as jnp
        import numpy as np
        D_MODEL = 256
        M = 64
        INNER = 16
        s = jnp.einsum('btd,dm->btm', x, Win) + bin_
        h = jax.nn.relu(s[..., None] * W1 + b1)
        g = jnp.einsum('btmh,mh->btm', h, W2) + b2
        out = jnp.einsum('btm,md->btd', g, Wout) + bout
        return out
    x = L0_attn_x
    x = x + _L0_attn_ref(_layernorm(x, axis=-1), L0_attn_ln_w, L0_attn_ln_b, L0_attn_w_xproj, L0_attn_w_dt, L0_attn_b_dt, L0_attn_A_log, L0_attn_Dp, L0_attn_w_out)
    x = x + _L0_ffn_ref(_layernorm(x, axis=-1), L0_ffn_Win, L0_ffn_bin_, L0_ffn_W1, L0_ffn_b1, L0_ffn_W2, L0_ffn_b2, L0_ffn_Wout, L0_ffn_bout)
    return x

_drawn_inputs = setup_inputs


def setup_inputs(seed=0):
    import zlib

    import numpy as np

    out = dict(_drawn_inputs(seed))
    spreads = {'L0_attn_ln_w': (1.0, 0.2),
     'L0_attn_ln_b': (0.0, 0.1),
     'L0_attn_b_dt': (0.0, 0.549),
     'L0_attn_Dp': (1.0, 0.2)}
    factors = {'L0_attn_w_dt': 7.14, 'L0_attn_A_log': 3.505, 'L0_ffn_bin_': 8.0}
    for name, (base, spread) in spreads.items():
        noise = np.random.default_rng([zlib.crc32(name.encode()), seed]).standard_normal(out[name].shape)
        drawn = base * np.exp(spread * noise) if base else spread * noise
        out[name] = jnp.asarray(drawn.astype(out[name].dtype))
    for name, factor in factors.items():
        out[name] = (out[name] * factor).astype(out[name].dtype)
    return out
```

```python
import concourse.bass as bass
from concourse import mybir
from contextlib import ExitStack

F32 = mybir.dt.float32
BF16 = mybir.dt.bfloat16
ALU = mybir.AluOpType
ACT = mybir.ActivationFunctionType
AX = mybir.AxisListType


class Signal:

    def __init__(self, handle, total):
        self.handle, self.total = handle, total


class Step:

    def __init__(self, i, like):
        self.i, self.like = i, like

    alone_on, long_done = (), None

    def wait(self, eng, signal, per_step, plus, alone=False):
        if isinstance(self.i, int):
            value = min(per_step * self.i + plus, signal.total)
            if value > 0:
                eng.wait_ge(signal.handle, value)
        else:
            assert per_step * self.like + plus >= 0
            value = self.i * per_step + plus
            if alone or eng in self.alone_on:
                value = eng.to_reg(value)
                eng.wait_ge(*self.long_done)
            eng.wait_ge(signal.handle, value)



def build(nc, x, ln_w, ln_b, w_xproj, w_dt, b_dt, A_log, Dp, w_out,
          Win, bin_, W1, b1, W2, b2, Wout, bout, out):
    TOKENS, D = x.shape
    P = 128
    H2 = D // P
    NS = A_log.shape[1]
    RANK = w_dt.shape[0]
    M, INNER = W2.shape[1], W2.shape[0] * W2.shape[2]
    SEQ = 512
    TILES = TOKENS // P
    TC = 64
    CHUNKS = TOKENS // TC
    SEQ_TILES = SEQ // P
    G = 4
    QD = P // G
    QT = TC // G
    TERMS = 9 * H2
    W = TC + 1
    UNITS = 8
    UC = P // UNITS
    UT = TC // UNITS
    NK = INNER // 2
    EPS = 1e-5
    LEAD, LAG = 2, 2
    assert H2 * NS == P and H2 * M == P and UC * TC == 1024

    ctx = ExitStack()
    with ctx:
        def sb(name, shape, dt=F32):
            return ctx.enter_context(nc.sbuf_tensor(name, shape, dt))

        def sig(name, total):
            return Signal(ctx.enter_context(nc.semaphore(name)), total)

        delta_dram = nc.dram_tensor("delta_parts", (TILES, TERMS, P * P), BF16, kind="Internal").ap()
        dx_dram = nc.dram_tensor("dx_parts", (TILES, TERMS, P * P), BF16, kind="Internal").ap()
        b_dram = nc.dram_tensor("b_parts", (TILES, TERMS, P * P), BF16, kind="Internal").ap()
        a_dram = nc.dram_tensor("a_parts", (1, TERMS, P * P), BF16, kind="Internal").ap()

        state = sb("state", [P, 2, P, W])
        decay = sb("decay", [P, 4, UC, W])
        a_rows = sb("a_rows", [P, QD, P], BF16)
        b_rows = sb("b_rows", [P, 2, QT, P], BF16)
        delta_rows = sb("delta_rows", [P, 2, G, QD // 2, TC], BF16)
        dx_rows = sb("dx_rows", [P, 2, G, QT, P], BF16)
        c_cols = sb("c_cols", [P, 2, TC, 32])
        x_in = sb("x_in", [P, D])
        x_ln = sb("x_ln", [P, D])
        x_hat = sb("x_hat", [P, D])
        xn_t = sb("xn_t", [P, H2, P])
        xd_t = sb("xd_t", [P, 4, H2, P])
        sp_t = sb("sp_t", [P, H2, P])
        sp_ln = sb("sp_ln", [P, H2, P])
        sp_e = sb("sp_e", [P, H2, P])
        sp_u = sb("sp_u", [P, H2, P])
        sp_c = sb("sp_c", [P, H2, P])
        sp_r = sb("sp_r", [P, H2, P])
        delta_parts = sb("delta_parts_sb", [P, H2, 3, P], BF16)
        dx_parts = sb("dx_parts_sb", [P, H2, 3, P], BF16)
        b_parts = sb("b_parts_sb", [P, 3, H2, P], BF16)
        dx_tok = sb("dx_tok", [P, H2, P])
        b_tok = sb("b_tok", [P, NS])
        c_t = sb("c_t", [P, 4, P])
        dtr_t = sb("dtr_t", [RANK, P])
        y_tok = sb("y_tok", [P, P])
        z_t = sb("z_t", [P, H2, P])
        x_res = sb("x_res", [P, D])
        x1 = sb("x1", [P, D])
        x1_ln = sb("x1_ln", [P, D])
        x1_t = sb("x1_t", [P, H2, P])
        s_t = sb("s_t", [P, P])
        hidden = sb("hidden", [P, NK, P])
        g_t = sb("g_t", [P, P])
        y_out = sb("y_out", [P, D])
        stats = sb("stats", [P, 3, 6])
        moments = sb("moments", [P, 3, 2])
        rstd = sb("rstd", [P, 3, 2])
        wx_sb = sb("wx_sb", [P, H2, RANK + NS])
        wc_sb = sb("wc_sb", [P, H2, P])
        wdt_sb = sb("wdt_sb", [RANK, D])
        wout_sb = sb("wout_sb", [P, H2, D])
        win_sb = sb("win_sb", [P, H2, P])
        fout_sb = sb("fout_sb", [P, D])
        bout_sb = sb("bout_sb", [1, D])
        ones_row = sb("ones_row", [1, P])
        ident = sb("ident", [P, P])
        w2_diag = sb("w2_diag", [P, NK, M])
        by_half = sb("by_half", [P, 4, H2])
        by_pair = sb("by_pair", [P, 3, NK])
        bin_sb = sb("bin_sb", [P, 1])
        b1w2 = sb("b1w2", [M, 2, INNER])
        g_bias = sb("g_bias", [P, 2])
        minus_half = sb("minus_half", [P, 1])

        def ps(name, shape):
            return ctx.enter_context(nc.psum_tensor(name, shape, F32))
        exponent_ps = ps("exponent_ps", [P, 1024])
        input_ps = ps("input_ps", [P, 1024])
        y_ps = ps("y_ps", [P, 512])
        tr_ps = ps("tr_ps", [P, 512])
        proj_ps = ps("proj_ps", [P, 512])
        post_ps = ps("post_ps", [P, 512])

        T, C = TILES, CHUNKS
        weights_loaded = sig("weights_loaded", 0)
        zeroed = sig("zeroed", 0)
        setup_dve = sig("setup_dve", 0)
        setup_act = sig("setup_act", 0)
        a_split = sig("a_split", 0)
        a_written = sig("a_written", 0)
        a_repeated = sig("a_repeated", 0)
        a_loaded = sig("a_loaded", 0)
        setup_done = sig("setup_done", 0)
        ident_zeroed = sig("ident_zeroed", 0)
        ident_made = sig("ident_made", 0)
        exponent_filled = sig("exponent_filled", UNITS * C)
        decay_made = sig("decay_made", UNITS * C)
        input_filled = sig("input_filled", UNITS * C)
        input_placed = sig("input_placed", UNITS * C)
        scanned = sig("scanned", UNITS * C)
        carried = sig("carried", 2 * C)
        y_summed = sig("y_summed", C)
        y_copied = sig("y_copied", C)
        y_turned = sig("y_turned", C)
        z_made = sig("z_made", C)
        c_placed = sig("c_placed", 2 * C)
        delta_loaded = [sig(f"delta_loaded{h}", 64 * C) for h in range(2)]
        rows_loaded = [sig(f"rows_loaded{k}", 128 * T) for k in range(2)]
        parts_written = sig("parts_written", 64 * T)
        parts_repeated = sig("parts_repeated", 96 * T)
        x_loaded = sig("x_loaded", 16 * T)
        normed = sig("normed", 6 * T)
        rstd_made = sig("rstd_made", 4 * T)
        x_turned = sig("x_turned", T)
        xn_made = sig("xn_made", 4 * T)
        projected = sig("projected", T)
        proj_copied = sig("proj_copied", 3 * T)
        dt_summed = sig("dt_summed", T)
        dt_biased = sig("dt_biased", 3 * T)
        e_made = sig("e_made", T)
        ln_made = sig("ln_made", T)
        r_made = sig("r_made", T)
        softplus_steps = sig("softplus_steps", 8 * T)
        delta_split = sig("delta_split", 5 * T)
        dx_turned = sig("dx_turned", T)
        dx_copied = sig("dx_copied", T)
        dx_split = sig("dx_split", 5 * T)
        b_split = sig("b_split", 6 * T)
        res_loaded = sig("res_loaded", 16 * T)
        mixed = sig("mixed", T)
        x1_steps = sig("x1_steps", 4 * T)
        rstd1_made = sig("rstd1_made", 2 * T)
        x1_turned = sig("x1_turned", T)
        x1_copied = sig("x1_copied", T)
        s_summed = sig("s_summed", T)
        hidden_steps = sig("hidden_steps", (1 + NK) * T)
        g_summed = sig("g_summed", T)
        g_made = sig("g_made", T)
        f_summed = sig("f_summed", T)
        out_made = sig("out_made", T)
        out_stored = sig("out_stored", 16 * T)

        def is_tile(j):
            return 0 <= j < TILES

        def is_chunk(c):
            return 0 <= c < CHUNKS

        def run_steps(eng, step, unroll):
            first, last = -LEAD, TILES + LAG
            lo = LAG + 1
            hi = lo + (TILES - LEAD - 1 - lo) // unroll * unroll
            for i in range(first, lo):
                step(Step(i, i))
            with eng.Fori(lo, hi, unroll) as base:
                for u in range(unroll):
                    step(Step(base + u if u else base, lo + u))
            for i in range(hi, last):
                step(Step(i, i))

        def moving_rows(dram):
            first = dram[:, 0:6, :].rearrange("o r (s x) -> s (o r) x", s=16)
            return first, [(dram[:, 6 * a:6 * a + 6, :].rearrange("o r (s x) -> s (o r) x", s=16), first)
                           for a in (1, 2)]

        def stationary_rows(dram):
            by_b = dram.rearrange("o (r b) x -> b (o r) x", b=3)
            first, second, third = (by_b[b].rearrange("r (s x) -> s r x", s=16) for b in range(3))
            return first, [(second, first), (third, first)]

        Step.alone_on, Step.long_done = [], (setup_done.handle, 1)
        block = ctx.enter_context(nc.Block())

        @block.sync
        def _(sp):
            Step.alone_on.append(sp)

            def load(dst, src):
                sp.dma_start(dst, src).then_inc(weights_loaded.handle, 16)
                weights_loaded.total += 16

            load(sp_t[:, :, 0:NS], A_log.rearrange("(h p) n -> p h n", h=H2))
            for n, v in enumerate((ln_w, ln_b, b_dt, Dp)):
                load(by_half[:, n, :], v.rearrange("p h -> p h"))
            load(wx_sb[:, :, :], w_xproj[:, 0:RANK + NS].rearrange("(h p) n -> p h n", h=H2))
            for h in range(H2):
                load(wc_sb[:, :, h * NS:(h + 1) * NS],
                     w_xproj[:, RANK + NS:RANK + 2 * NS].rearrange("(h p) n -> p h n", h=H2))
                load(win_sb[:, :, h * M:(h + 1) * M], Win.rearrange("(h p) m -> p h m", h=H2))
                load(fout_sb[h * M:(h + 1) * M, :], Wout)
                load(bin_sb[h * M:(h + 1) * M, :], bin_)
            load(wdt_sb[:, :], w_dt)
            load(wout_sb[:, :, :], w_out.rearrange("(h p) n -> p h n", h=H2))
            load(bout_sb[:, :], bout)
            for n, v in enumerate((W1, b1, W2)):
                for a in range(2):
                    load(by_pair[a * M:(a + 1) * M, n, :], v[a])
            for n, v in enumerate((b1, W2)):
                for a in range(2):
                    load(b1w2[:, n, a * NK:(a + 1) * NK], v[a])
            load(g_bias[0:M, 0:1], b2)
            sp.wait_ge(a_split.handle, 1)
            sp.dma_start(a_dram.rearrange("o (r b) (p c) -> b p (o r) c", b=3, c=P)[0],
                         b_parts[:, :, :, :].rearrange("p a h c -> p (a h) c")).then_inc(a_written.handle, 16)
            sp.wait_ge(a_written.handle, 16)
            for dst, src in stationary_rows(a_dram)[1]:
                sp.dma_start(dst, src).then_inc(a_repeated.handle, 16)
            sp.wait_ge(a_repeated.handle, 32)
            sp.wait_ge(zeroed.handle, 1)

            for g in range(G):
                sp.dma_start(a_rows[32 * g:32 * g + TERMS, :, :].rearrange("p q c -> p (q c)"),
                             a_dram[0, :, g * QD * P:(g + 1) * QD * P]).then_inc(a_loaded.handle, 16)

            def load_delta(st, k, half):
                if not is_chunk(2 * st.like + k):
                    return
                st.wait(sp, exponent_filled, 16, 8 * (k - 1) + 4 * (half + 1))
                for g in range(G):
                    lo = k * P * TC + (g * QD + half * (QD // 2)) * TC
                    sp.dma_start(delta_rows[32 * g:32 * g + TERMS, half, g, :, :].rearrange("p q t -> p (q t)"),
                                 delta_dram[bass.ds(st.i, 1), :, lo:lo + QD // 2 * TC]
                                 .rearrange("o r x -> (o r) x")).then_inc(delta_loaded[half].handle, 16)

            def load_input(st, k):
                if not is_chunk(2 * st.like + 2 + k):
                    return
                st.wait(sp, input_filled, 16, 8 * k + 8)
                tile = bass.ds(st.i + 1, 1)
                for g in range(G):
                    lo = (k * TC + g * QT) * P
                    for buf, dram in ((dx_rows[32 * g:32 * g + TERMS, k, g, :, :], dx_dram),
                                      (b_rows[32 * g:32 * g + TERMS, k, :, :], b_dram)):
                        sp.dma_start(buf.rearrange("p q c -> p (q c)"),
                                     dram[tile, :, lo:lo + QT * P].rearrange("o r x -> (o r) x")
                                     ).then_inc(rows_loaded[k].handle, 16)

            def step(st):
                i, r = st.i, st.like
                load_delta(st, 1, 0)
                if is_tile(r + 1):
                    st.wait(sp, delta_split, 5, 10)
                    st.wait(sp, dx_split, 5, 10)
                    st.wait(sp, b_split, 6, 12)
                    tile = bass.ds(i + 1, 1)
                    for k in range(2):
                        sp.dma_start(
                            delta_dram[tile, 0:6, k * P * TC:(k + 1) * P * TC]
                            .rearrange("o r (p t) -> p (o r) t", t=TC),
                            delta_parts[:, :, :, k * TC:(k + 1) * TC].rearrange("p h a t -> p (h a) t")
                        ).then_inc(parts_written.handle, 16)
                    sp.dma_start(dx_dram[tile, 0:6, :].rearrange("o r (p c) -> p (o r) c", c=P),
                                 dx_parts[:, :, :, :].rearrange("p h a c -> p (h a) c")
                                 ).then_inc(parts_written.handle, 16)
                    sp.dma_start(b_dram[tile, :, :].rearrange("o (r b) (p c) -> b p (o r) c", b=3, c=P)[0],
                                 b_parts[:, :, :, :].rearrange("p a h c -> p (a h) c")
                                 ).then_inc(parts_written.handle, 16)
                    st.wait(sp, parts_written, 64, 128)
                    for form, dram in ((moving_rows, delta_dram), (moving_rows, dx_dram), (stationary_rows, b_dram)):
                        for dst, src in form(dram[tile, :, :])[1]:
                            sp.dma_start(dst, src).then_inc(parts_repeated.handle, 16)
                    st.wait(sp, parts_repeated, 96, 192)
                    load_input(st, 0)
                load_delta(st, 1, 1)
                if r == -LEAD:
                    sp.dma_start(x_in[:, :], x[0:P, :]).then_inc(x_loaded.handle, 16)
                if is_tile(r + 3):
                    st.wait(sp, normed, 6, 18 - 3)
                    sp.dma_start(x_in[:, :], x[bass.ds(i * P + 3 * P, P), :]).then_inc(x_loaded.handle, 16)
                if is_tile(r - 1):
                    st.wait(sp, x1_steps, 4, 4 * (-2) + 1)
                    sp.dma_start(x_res[:, :], x[bass.ds(i * P - P, P), :]).then_inc(res_loaded.handle, 16)
                load_input(st, 1)
                load_delta(Step(i + 1, r + 1), 0, 0)
                if is_tile(r - 2):
                    st.wait(sp, out_made, 1, -1)
                    sp.dma_start(out[bass.ds(i * P - 2 * P, P), :], y_out[:, :]).then_inc(out_stored.handle, 16)
                load_delta(Step(i + 1, r + 1), 0, 1)

            run_steps(sp, step, 1)
            sp.wait_ge(out_stored.handle, out_stored.total)
            for written in (parts_written, parts_repeated):
                sp.wait_ge(written.handle, written.total)

        @block.tensor
        def _(pe):
            mm = pe.matmul
            pe.wait_ge(setup_done.handle, 1)
            pe.wait_ge(a_loaded.handle, 16 * G)

            def exponent(st, k, s):
                st.wait(pe, decay_made, 16, 8 * k + s)
                if s % 4 == 0:
                    st.wait(pe, delta_loaded[s // 4], 128, 64 * (k + 1))
                for q in range(4 * s, 4 * s + 4):
                    last = mm(exponent_ps[:, (q % 4) * G * TC:(q % 4 + 1) * G * TC], a_rows[:, q, :],
                              delta_rows[:, s // 4, :, q % (QD // 2), :], start=True, stop=True)
                last.then_inc(exponent_filled.handle, 1)

            def scan_input(st, k, s):
                kn = (k + 1) % 2
                st.wait(pe, input_placed, 16, 8 * (k + 1) + s)
                if s == 0:
                    st.wait(pe, rows_loaded[kn], 128, 128 * (k + 1))
                for n in range(2):
                    q = 2 * s + n
                    last = mm(input_ps[:, n * 512:(n + 1) * 512], b_rows[:, kn, q, :],
                              dx_rows[:, kn, :, q, :], start=True, stop=True)
                last.then_inc(input_filled.handle, 1)

            def y_sum(st, k, s):
                kp = (k + 1) % 2
                if s == 0:
                    st.wait(pe, scanned, 16, 8 * k)
                    st.wait(pe, c_placed, 4, 2 * k)
                    st.wait(pe, y_copied, 2, k - 1)
                for n in range(2):
                    for g in range(G):
                        t = QT * g + 2 * s + n
                        last = mm(y_ps[32 * g:32 * g + 32, 0:P], c_cols[:, kp, t, :], state[:, kp, :, 1 + t],
                                  start=(s == 0 and n == 0), stop=(s == UNITS - 1 and n == 1))
                if s == UNITS - 1:
                    last.then_inc(y_summed.handle, 1)

            def step(st):
                r = st.like
                for k in range(2):
                    for s in range(UNITS):
                        if is_chunk(2 * r + k):
                            exponent(st, k, s)
                        if is_chunk(2 * r + k - 1):
                            y_sum(st, k, s)
                        if is_chunk(2 * r + k + 1):
                            scan_input(st, k, s)
                        if s == 1 and is_chunk(2 * r + k - 2):
                            st.wait(pe, y_copied, 2, k - 1)
                            if k == 0:
                                st.wait(pe, dx_copied, 1, 2)
                            else:
                                st.wait(pe, proj_copied, 3, 9)
                            pe.transpose(proj_ps[:, 0:P], y_tok[:, :], ident[:, :]).then_inc(y_turned.handle, 1)
                        if is_tile(r + 2):
                            prepare(st, k, s)
                        if is_tile(r - 2) and k == 0:
                            mlp(st, s)
                        if is_tile(r - 1) and (k, s) == (1, 4):
                            st.wait(pe, z_made, 2, 0)
                            st.wait(pe, out_made, 1, -1)
                            for h in range(H2):
                                last = mm(post_ps[:, 0:D], z_t[:, h, :], wout_sb[:, h, :],
                                          start=(h == 0), stop=(h == H2 - 1))
                            last.then_inc(mixed.handle, 1)

            def prepare(st, k, s):
                if (k, s) == (0, 3):
                    st.wait(pe, normed, 6, 18)
                    st.wait(pe, dt_biased, 3, 6)
                    for n, src in enumerate((x_ln, x_hat)):
                        for h in range(H2):
                            last = pe.transpose(tr_ps[:, (2 * n + h) * P:(2 * n + h + 1) * P],
                                                src[:, h * P:(h + 1) * P], ident[:, :])
                    last.then_inc(x_turned.handle, 1)
                if (k, s) == (0, 5):
                    st.wait(pe, xn_made, 4, 12)
                    st.wait(pe, z_made, 2, -1)
                    for dst, lhs, rhs in (
                            (proj_ps[0:RANK, 0:P], lambda h: wx_sb[:, h, 0:RANK], lambda h: xn_t[:, h, :]),
                            (proj_ps[:, P:P + NS], lambda h: xn_t[:, h, :], lambda h: wx_sb[:, h, RANK:RANK + NS]),
                            (proj_ps[:, 2 * P:3 * P], lambda h: wc_sb[:, h, :], lambda h: xn_t[:, h, :])):
                        for h in range(H2):
                            last = mm(dst, lhs(h), rhs(h), start=(h == 0), stop=(h == H2 - 1))
                    last.then_inc(projected.handle, 1)
                if (k, s) == (0, 7):
                    st.wait(pe, proj_copied, 3, 9)
                    for h in range(H2):
                        last = mm(tr_ps[:, h * P:(h + 1) * P], wdt_sb[:, h * P:(h + 1) * P], dtr_t[:, :],
                                  start=True, stop=True)
                    last.then_inc(dt_summed.handle, 1)
                if (k, s) == (1, 7):
                    st.wait(pe, softplus_steps, 8, 24)
                    st.wait(pe, z_made, 2, 0)
                    for h in range(H2):
                        last = pe.transpose(proj_ps[:, h * P:(h + 1) * P], sp_e[:, h, :], ident[:, :])
                    last.then_inc(dx_turned.handle, 1)

            def mlp(st, s):
                if s == 0:
                    st.wait(pe, x1_steps, 4, -4)
                    for h in range(H2):
                        last = pe.transpose(post_ps[:, h * P:(h + 1) * P], x1_ln[:, h * P:(h + 1) * P], ident[:, :])
                    last.then_inc(x1_turned.handle, 1)
                if s == 2:
                    st.wait(pe, x1_copied, 1, -1)
                    for h in range(H2):
                        last = mm(post_ps[:, 0:P], win_sb[:, h, :], x1_t[:, h, :], start=(h == 0), stop=(h == H2 - 1))
                    last.then_inc(s_summed.handle, 1)
                if s == 5:
                    st.wait(pe, hidden_steps, 1 + NK, -(1 + NK))
                    for n in range(NK):
                        half = n % 2
                        last = mm(post_ps[half * M:(half + 1) * M, 0:P], w2_diag[:, n, :], hidden[:, n, :],
                                  start=(n < 2), stop=(n >= NK - 2))
                    last.then_inc(g_summed.handle, 1)
                if s == 7:
                    st.wait(pe, g_made, 1, -1)
                    mm(post_ps[:, 0:D], g_t[:, :], fout_sb[:, :], start=True, stop=False)
                    mm(post_ps[:, 0:D], ones_row[:, :], bout_sb[:, :], start=False, stop=True)\
                        .then_inc(f_summed.handle, 1)

            run_steps(pe, step, 1)

        @block.scalar
        def _(act):
            act.preload_act_table_set("natural_log_exp_and_others")
            act.wait_ge(weights_loaded.handle, weights_loaded.total)
            act.activation(sp_e[:, :, 0:NS], sp_t[:, :, 0:NS], ACT.Exp).then_inc(setup_act.handle, 1)
            act.wait_ge(setup_done.handle, 1)

            def step(st):
                r = st.like
                for k in range(2):
                    for s in range(UNITS):
                        if is_chunk(2 * r + k):
                            st.wait(act, exponent_filled, 16, 8 * k + s + 1)
                            st.wait(act, scanned, 16, 8 * k + s + 1 - 4)
                            act.activation(decay[:, s % 4, :, 1:W],
                                           exponent_ps[:, :].rearrange("p (d t) -> p d t", t=TC),
                                           ACT.Exp).then_inc(decay_made.handle, 1)
                        if is_chunk(2 * r + k + 1):
                            st.wait(act, input_filled, 16, 8 * (k + 1) + s + 1)
                            if s == UNITS - 1:
                                st.wait(act, carried, 4, 2 * k + 2)
                            dst = state[:, (k + 1) % 2, :, 1:W].rearrange("p d (g q) -> p q g d", g=G)
                            act.activation(dst[:, 2 * s:2 * s + 2, :, :],
                                           input_ps[:, :].rearrange("p (q g d) -> p q g d", q=2, g=G),
                                           ACT.Copy).then_inc(input_placed.handle, 1)
                        if is_tile(r + 2) and (k, s) == (1, 1):
                            st.wait(act, dt_biased, 3, 9)
                            st.wait(act, dx_turned, 1, 2)
                            act.activation(sp_e[:, :, :], sp_ln[:, :, :], ACT.Exp).then_inc(e_made.handle, 1)
                        if is_tile(r + 2) and (k, s) == (1, 3):
                            st.wait(act, softplus_steps, 8, 8 * 2 + 1)
                            act.activation(sp_ln[:, :, :], sp_u[:, :, :], ACT.Ln).then_inc(ln_made.handle, 1)

            run_steps(act, step, 1)

        @block.vector
        def _(dve):
            dve.wait_ge(setup_act.handle, 1)
            dve.wait_ge(zeroed.handle, 1)
            own = [0]

            def then(ins):
                own[0] += 1
                ins.then_inc(setup_dve.handle, 1)
                dve.wait_ge(setup_dve.handle, own[0])

            rest = sp_e[:, :, 0:NS]
            then(dve.tensor_scalar(rest, rest, -1.0, None, ALU.mult))
            for a in range(3):
                for h in range(H2):
                    part = b_parts[:, a, h, h * NS:(h + 1) * NS]
                    then(dve.tensor_copy(part, sp_e[:, h, 0:NS]))
                    if a < 2:
                        then(dve.tensor_tensor(sp_e[:, h, 0:NS], sp_e[:, h, 0:NS], part, ALU.subtract))
            dve.memset(minus_half[:, :], -0.5).then_inc(a_split.handle, 1)
            dve.wait_ge(weights_loaded.handle, weights_loaded.total)
            then(dve.tensor_scalar(by_pair[:, 1, :], by_pair[:, 1, :], -1.0, None, ALU.mult))
            dve.wait_ge(ident_made.handle, 1)
            for n in range(NK):
                then(dve.tensor_tensor(w2_diag[:, n, :], ident[:, 0:M], ident[:, M:2 * M], ALU.add))
                then(dve.tensor_scalar(w2_diag[:, n, :], w2_diag[:, n, :], by_pair[:, 2, n:n + 1], None, ALU.mult))
            then(dve.tensor_tensor(b1w2[:, 0, :], b1w2[:, 0, :], b1w2[:, 1, :], ALU.mult))
            then(dve.reduce_sum(g_bias[0:M, 1:2], b1w2[:, 0, :], axis=AX.X))
            then(dve.tensor_tensor(g_bias[0:M, 0:1], g_bias[0:M, 0:1], g_bias[0:M, 1:2], ALU.add))
            then(dve.memset(g_bias[M:P, 0:1], 0.0))
            then(dve.memset(ones_row[:, :], 1.0))
            dve.wait_ge(a_written.handle, 16)
            dve.engine_nop().then_inc(setup_done.handle, 1)

            def step(st):
                r = st.like
                for k in range(2):
                    for s in range(UNITS):
                        if is_chunk(2 * r + k):
                            st.wait(dve, decay_made, 16, 8 * k + s + 1)
                            if s == 0:
                                st.wait(dve, input_placed, 16, 8 * k + 8)
                            if s % 4 == 0:
                                st.wait(dve, carried, 4, 2 * k + 1 + s // 4)
                            stretch = state[:, k, UC * s:UC * (s + 1), :].rearrange("p d t -> p (d t)")
                            dve.tensor_tensor_scan(stretch, decay[:, s % 4, :, :].rearrange("p d t -> p (d t)"),
                                                   stretch, 0.0, ALU.mult, ALU.add).then_inc(scanned.handle, 1)
                        if s == 7 and is_chunk(2 * r + k - 1):
                            st.wait(dve, y_summed, 2, k)
                            st.wait(dve, y_turned, 2, k - 1)
                            dve.tensor_copy(y_tok[:, :].rearrange("p (g q) -> p g q", g=G),
                                            y_ps[:, 0:P].rearrange("p (q g) -> p g q", g=G)
                                            ).then_inc(y_copied.handle, 1)
                        if s == 2 and is_chunk(2 * r + k - 2):
                            st.wait(dve, y_turned, 2, k - 1)
                            st.wait(dve, mixed, 1, -1)
                            dve.tensor_tensor(z_t[:, :, k * TC:(k + 1) * TC],
                                              proj_ps[:, 0:P].rearrange("p (t h) -> p h t", h=H2),
                                              xd_t[:, (r - 1) % 4, :, k * TC:(k + 1) * TC],
                                              ALU.add).then_inc(z_made.handle, 1)
                        if is_tile(r + 1) and (k, s) == (0, 0):
                            st.wait(dve, dx_turned, 1, 2)
                            st.wait(dve, dx_split, 5, 5)
                            dve.tensor_copy(dx_tok[:, :, :].rearrange("p h (q g) -> p h q g", g=G),
                                            proj_ps[:, 0:D].rearrange("p (h g q) -> p h q g", h=H2, g=G)
                                            ).then_inc(dx_copied.handle, 1)
                        if s == 5:
                            place_c(st, k)
                        if is_tile(r + 2):
                            prepare(st, k, s)
                        if is_tile(r - 2):
                            mlp(st, k, s)
                        if is_tile(r - 1) and k == 1:
                            residual(st, s)

            def place_c(st, k):
                if not is_chunk(2 * st.like + k):
                    return
                st.wait(dve, y_summed, 2, k - 1)
                st.wait(dve, proj_copied, 3, 3)
                for h in range(H2):
                    rows = slice(h * NS, (h + 1) * NS)
                    dst = c_cols[rows, k, :, :].rearrange("p (g q) c -> p g (q c)", g=G)
                    dve.tensor_copy(dst[:, :, h:h + 34 * (QT - 1) + 1:34],
                                     c_t[rows, st.like % 4, k * TC:(k + 1) * TC]
                                     .rearrange("p (g q) -> p g q", g=G)).then_inc(c_placed.handle, 1)

            def prepare(st, k, s):
                if (k, s) == (0, 0):
                    st.wait(dve, x_loaded, 16, 48)
                    dve.bn_stats(stats[:, 0, :], x_in[:, :]).then_inc(normed.handle, 1)
                    st.wait(dve, normed, 6, 13, alone=True)
                    dve.bn_aggr(moments[:, 0, :], stats[:, 0, :]).then_inc(normed.handle, 1)
                if (k, s) == (0, 1):
                    st.wait(dve, rstd_made, 4, 10)
                    st.wait(dve, x_turned, 1, 2)
                    dve.tensor_scalar(x_ln[:, :], x_in[:, :], moments[:, 0, 0:1], rstd[:, 0, 1:2],
                                      ALU.subtract, ALU.mult).then_inc(normed.handle, 1)
                    st.wait(dve, normed, 6, 15)
                    dve.bn_stats(stats[:, 1, :], x_ln[:, :]).then_inc(normed.handle, 1)
                    st.wait(dve, normed, 6, 16, alone=True)
                    dve.bn_aggr(moments[:, 1, :], stats[:, 1, :]).then_inc(normed.handle, 1)
                if (k, s) == (0, 2):
                    st.wait(dve, rstd_made, 4, 12)
                    dve.tensor_scalar(x_hat[:, :], x_ln[:, :], moments[:, 1, 0:1], rstd[:, 1, 1:2],
                                      ALU.subtract, ALU.mult).then_inc(normed.handle, 1)
                if (k, s) == (0, 4):
                    st.wait(dve, x_turned, 1, 3)
                    st.wait(dve, softplus_steps, 8, 16)
                    for h in range(H2):
                        dve.tensor_scalar(xd_t[:, (st.like + 2) % 4, h, :], tr_ps[:, h * P:(h + 1) * P],
                                          by_half[:, 3, h:h + 1], None, ALU.mult).then_inc(xn_made.handle, 1)
                        dve.tensor_scalar(xn_t[:, h, :], tr_ps[:, (2 + h) * P:(3 + h) * P],
                                          by_half[:, 0, h:h + 1], by_half[:, 1, h:h + 1],
                                          ALU.mult, ALU.add).then_inc(xn_made.handle, 1)
                if (k, s) == (0, 6):
                    st.wait(dve, projected, 1, 3)
                    st.wait(dve, b_split, 6, 12)
                    dve.tensor_copy(dtr_t[:, :], proj_ps[0:RANK, 0:P]).then_inc(proj_copied.handle, 1)
                    dve.tensor_copy(b_tok[:, :], proj_ps[:, P:P + NS]).then_inc(proj_copied.handle, 1)
                    dve.tensor_copy(c_t[:, (st.like + 2) % 4, :], proj_ps[:, 2 * P:3 * P])\
                       .then_inc(proj_copied.handle, 1)
                if (k, s) == (1, 0):
                    st.wait(dve, dt_summed, 1, 3)
                    st.wait(dve, delta_split, 5, 10)
                    for h in range(H2):
                        dve.tensor_scalar(sp_t[:, h, :], tr_ps[:, h * P:(h + 1) * P], by_half[:, 2, h:h + 1],
                                          None, ALU.add).then_inc(dt_biased.handle, 1)
                    st.wait(dve, dt_biased, 3, 8)
                    dve.scalar_tensor_tensor(sp_ln[:, :, :], sp_t[:, :, :], -1.0, sp_t[:, :, :],
                                             ALU.mult, ALU.min).then_inc(dt_biased.handle, 1)
                if (k, s) == (1, 3):
                    st.wait(dve, softplus_steps, 8, 17)
                    dve.reciprocal(sp_r[:, :, :], sp_u[:, :, :]).then_inc(r_made.handle, 1)

            def residual(st, s):
                if s == 5:
                    st.wait(dve, mixed, 1, 0)
                    st.wait(dve, res_loaded, 16, 0)
                    dve.tensor_tensor(x1[:, :], post_ps[:, 0:D], x_res[:, :], ALU.add).then_inc(x1_steps.handle, 1)
                    st.wait(dve, x1_steps, 4, -3)
                    dve.bn_stats(stats[:, 2, :], x1[:, :]).then_inc(x1_steps.handle, 1)
                    st.wait(dve, x1_steps, 4, -2, alone=True)
                    dve.bn_aggr(moments[:, 2, :], stats[:, 2, :]).then_inc(x1_steps.handle, 1)
                if s == 7:
                    st.wait(dve, rstd1_made, 2, 0)
                    dve.tensor_scalar(x1_ln[:, :], x1[:, :], moments[:, 2, 0:1], rstd[:, 2, 1:2],
                                      ALU.subtract, ALU.mult).then_inc(x1_steps.handle, 1)

            def mlp(st, k, s):
                if (k, s) == (0, 1):
                    st.wait(dve, x1_turned, 1, -1)
                    dve.tensor_copy(x1_t[:, :, :], post_ps[:, 0:D].rearrange("p (h t) -> p h t", h=H2))\
                       .then_inc(x1_copied.handle, 1)
                if (k, s) == (0, 3):
                    st.wait(dve, s_summed, 1, -1)
                    dve.tensor_scalar(s_t[:, :], post_ps[:, 0:P], bin_sb[:, 0:1], None, ALU.add)\
                       .then_inc(hidden_steps.handle, 1)
                    st.wait(dve, hidden_steps, 1 + NK, -2 * (1 + NK) + 1)
                    for n in range(NK):
                        dve.tensor_scalar(hidden[:, n, :], s_t[:, :], by_pair[:, 0, n:n + 1],
                                          by_pair[:, 1, n:n + 1], ALU.mult, ALU.max).then_inc(hidden_steps.handle, 1)
                if (k, s) == (0, 6):
                    st.wait(dve, g_summed, 1, -1)
                    dve.tensor_scalar(g_t[:, :], post_ps[:, 0:P], g_bias[:, 0:1], None, ALU.add)\
                       .then_inc(g_made.handle, 1)
                if (k, s) == (1, 0):
                    st.wait(dve, f_summed, 1, -1)
                    st.wait(dve, out_stored, 16, 16 * -2)
                    dve.tensor_tensor(y_out[:, :], post_ps[:, 0:D], x1[:, :], ALU.add).then_inc(out_made.handle, 1)

            run_steps(dve, step, 4)

        @block.gpsimd
        def _(pool):
            Step.alone_on.append(pool)
            pool.memset(ident[:, :], 0.0).then_inc(ident_zeroed.handle, 1)
            pool.wait_ge(ident_zeroed.handle, 1)
            pool.affine_select(out=ident[:, :], in_=ident[:, :], compare_op=ALU.not_equal, fill=1.0, base=0,
                               pattern=[[-1, P]], channel_multiplier=1).then_inc(ident_made.handle, 1)
            for z in (a_rows[:, :, :], b_rows[:, :, :, :], delta_rows[:, :, :, :, :], dx_rows[:, :, :, :, :],
                      c_cols[:, :, :, :], decay[:, :, :, 0]):
                pool.memset(z, 0.0)
            pool.memset(b_parts[:, :, :, :], 0.0).then_inc(zeroed.handle, 1)
            for half in range(2):
                pool.memset(state[:, 0, 64 * half:64 * (half + 1), 0], 0.0).then_inc(carried.handle, 1)
            pool.wait_ge(setup_done.handle, 1)

            def carry(st, k, half):
                c = 2 * st.like + k
                if not (is_chunk(c) and is_chunk(c + 1)):
                    return
                ch = slice(64 * half, 64 * (half + 1))
                st.wait(pool, scanned, 16, 8 * k + 4 * (half + 1))
                dst = state[:, (k + 1) % 2, ch, 0]
                if k == 1 and st.like % SEQ_TILES == SEQ_TILES - 1:
                    pool.memset(dst, 0.0).then_inc(carried.handle, 1)
                else:
                    pool.tensor_copy(dst, state[:, k, ch, W - 1]).then_inc(carried.handle, 1)

            def rstd_of(st, n, signal, per, at):
                pool.tensor_scalar(rstd[:, n, 0:1], moments[:, n, 1:2], EPS, None, ALU.add).then_inc(signal.handle, 1)
                st.wait(pool, signal, per, at + 1)
                pool.tensor_tensor(rstd[:, n, 1:2], rstd[:, n, 0:1], minus_half[:, :], ALU.pow)\
                    .then_inc(signal.handle, 1)

            def split(st, rest, parts, signal, per, at):
                for a in range(3):
                    if a:
                        st.wait(pool, signal, per, at + 2 * a)
                    pool.tensor_copy(parts[a], rest).then_inc(signal.handle, 1)
                    if a < 2:
                        st.wait(pool, signal, per, at + 2 * a + 1)
                        pool.tensor_tensor(rest, rest, parts[a], ALU.subtract).then_inc(signal.handle, 1)

            def step(st):
                r = st.like
                if is_tile(r + 2):
                    st.wait(pool, normed, 6, 14)
                    rstd_of(st, 0, rstd_made, 4, 8)
                if is_tile(r + 2):
                    st.wait(pool, normed, 6, 17)
                    rstd_of(st, 1, rstd_made, 4, 10)
                if is_tile(r + 1):
                    st.wait(pool, dx_copied, 1, 2)
                    st.wait(pool, parts_written, 64, 64)
                    split(st, dx_tok[:, :, :], [dx_parts[:, :, a, :] for a in range(3)], dx_split, 5, 5)
                carry(st, 0, 0)
                carry(st, 0, 1)
                if is_tile(r + 2):
                    st.wait(pool, proj_copied, 3, 9)
                    st.wait(pool, parts_written, 64, 128)
                    split(st, b_tok[:, :], [b_parts[:, a, 0, 0:NS] for a in range(3)], b_split, 6, 12)
                    st.wait(pool, b_split, 6, 17)
                    pool.tensor_copy(b_parts[:, :, 1, NS:2 * NS], b_parts[:, :, 0, 0:NS]).then_inc(b_split.handle, 1)
                    S, sps = softplus_steps.handle, softplus_steps
                    st.wait(pool, e_made, 1, 3)
                    pool.tensor_scalar(sp_u[:, :, :], sp_e[:, :, :], 1.0, None, ALU.add).then_inc(S, 1)
                    st.wait(pool, sps, 8, 17)
                    pool.tensor_scalar(sp_c[:, :, :], sp_u[:, :, :], -1.0, None, ALU.add).then_inc(S, 1)
                    st.wait(pool, sps, 8, 18)
                    pool.tensor_tensor(sp_c[:, :, :], sp_c[:, :, :], sp_e[:, :, :], ALU.subtract).then_inc(S, 1)
                    pool.tensor_scalar(sp_t[:, :, :], sp_t[:, :, :], 0.0, None, ALU.max).then_inc(S, 1)
                carry(st, 1, 0)
                if is_tile(r + 2):
                    st.wait(pool, r_made, 1, 3)
                    st.wait(pool, sps, 8, 20)
                    pool.tensor_tensor(sp_c[:, :, :], sp_c[:, :, :], sp_r[:, :, :], ALU.mult).then_inc(S, 1)
                    st.wait(pool, ln_made, 1, 3)
                    st.wait(pool, sps, 8, 21)
                    pool.tensor_tensor(sp_c[:, :, :], sp_ln[:, :, :], sp_c[:, :, :], ALU.subtract).then_inc(S, 1)
                    st.wait(pool, sps, 8, 22)
                    pool.tensor_tensor(sp_t[:, :, :], sp_t[:, :, :], sp_c[:, :, :], ALU.add).then_inc(S, 1)
                    st.wait(pool, sps, 8, 23)
                    pool.tensor_tensor(sp_e[:, :, :], sp_t[:, :, :], xn_t[:, :, :], ALU.mult).then_inc(S, 1)
                if is_tile(r - 1):
                    st.wait(pool, x1_steps, 4, -1)
                    rstd_of(st, 2, rstd1_made, 2, -2)
                if is_tile(r + 2):
                    st.wait(pool, sps, 8, 24)
                    st.wait(pool, parts_written, 64, 128)
                    split(st, sp_t[:, :, :], [delta_parts[:, :, a, :] for a in range(3)], delta_split, 5, 10)
                carry(st, 1, 1)

            run_steps(pool, step, 4)


def kernel(L0_attn_x, L0_attn_ln_w, L0_attn_ln_b, L0_attn_w_xproj, L0_attn_w_dt, L0_attn_b_dt, L0_attn_A_log,
           L0_attn_Dp, L0_attn_w_out, L0_ffn_Win, L0_ffn_bin_, L0_ffn_W1, L0_ffn_b1, L0_ffn_W2, L0_ffn_b2,
           L0_ffn_Wout, L0_ffn_bout):
    import numpy as np
    import concourse.bacc as bacc
    from concourse.bass_utils import run_bass_kernel_spmd

    def halves(v):
        return np.asarray(v).reshape(2, 128).T

    def inner_pairs(v):
        m, inner = v.shape
        return np.asarray(v).reshape(m, inner // 2, 2).transpose(2, 0, 1)

    x = np.asarray(L0_attn_x)
    arrays = {
        "x": x.reshape(-1, x.shape[-1]),
        "ln_w": halves(L0_attn_ln_w), "ln_b": halves(L0_attn_ln_b),
        "w_xproj": L0_attn_w_xproj, "w_dt": L0_attn_w_dt, "b_dt": halves(L0_attn_b_dt),
        "A_log": L0_attn_A_log, "Dp": halves(L0_attn_Dp), "w_out": L0_attn_w_out,
        "Win": L0_ffn_Win, "bin_": np.asarray(L0_ffn_bin_).reshape(-1, 1),
        "W1": inner_pairs(L0_ffn_W1), "b1": inner_pairs(L0_ffn_b1), "W2": inner_pairs(L0_ffn_W2),
        "b2": np.asarray(L0_ffn_b2).reshape(-1, 1), "Wout": L0_ffn_Wout,
        "bout": np.asarray(L0_ffn_bout).reshape(1, -1),
    }
    arrays = {f"in_{name}": np.ascontiguousarray(v) for name, v in arrays.items()}
    nc = bacc.Bacc("TRN2", target_bir_lowering=False, num_devices=1)
    args = [nc.dram_tensor(name, v.shape, mybir.dt.from_np(v.dtype), kind="ExternalInput").ap()
            for name, v in arrays.items()]
    args.append(nc.dram_tensor("out", arrays["in_x"].shape, F32, kind="ExternalOutput").ap())
    build(nc, *args)
    result = run_bass_kernel_spmd(nc, [arrays], core_ids=[0])
    return result.results[0]["out"].reshape(x.shape)
```
